# Optimizing a Trainium2 kernel written in Bass

```python
import numpy as np
import jax
import jax.numpy as jnp

def _softmax(x, axis=-1):
    return jax.nn.softmax(x, axis=axis)

def _gelu(x):
    return jax.nn.gelu(x, approximate=True)

def _silu(x):
    return jax.nn.silu(x)

def _sigmoid(x):
    return jax.nn.sigmoid(x)

def _layernorm(x, axis=-1, eps=1e-05):
    m = jnp.mean(x, axis=axis, keepdims=True)
    v = jnp.var(x, axis=axis, keepdims=True)
    return (x - m) / jnp.sqrt(v + eps)

def _scatter_add(tgt, idx, src, axis=0):
    return tgt.at[idx].add(src)

def _segment_sum(src, seg, n):
    return jax.ops.segment_sum(src, seg, n)
kernel_name = 'mk_gnn_preln_d2_gnn_r8_32d1f5'

def setup_inputs(seed: int=0):
    np.random.seed(seed)
    _w = jnp.asarray

    def _rec_inputs():
        import jax
        import jax.numpy as jnp
        _gk = jax.random.key(seed)
        x = -0.0006008 + 1.001 * jax.random.normal(jax.random.fold_in(_gk, 1), (12500, 128), jnp.float32)
        src = jax.random.randint(jax.random.fold_in(_gk, 2), (200000,), 0, 12500, jnp.int32)
        dst = jax.random.randint(jax.random.fold_in(_gk, 3), (200000,), 0, 12500, jnp.int32)
        _o = jnp.argsort(dst, stable=True)
        src = src[_o]
        dst = dst[_o]
        edge_type_4 = jax.random.randint(jax.random.fold_in(_gk, 12), (200000,), 0, 4, jnp.int32)
        edge_weight = jax.random.uniform(jax.random.fold_in(_gk, 13), (200000,), jnp.float32, 0.0, 0.999996)
        return (x, src, dst, edge_type_4, edge_weight)
    x, src, dst, edge_type_4, edge_weight = _rec_inputs()

    def _L0_gnn_setup():
        import jax, jax.numpy as jnp
        import numpy as np
        NUM_RELATIONS = 4
        N_NODES = 2500
        N_EDGES = 40000
        F_IN = 128
        HID = 128
        EMB = 128

        def _rgcn_conv(x, src, dst, edge_type, edge_weight, W, root, bias):
            xj = x[src]
            m = jnp.zeros((xj.shape[0], W.shape[2]), dtype=x.dtype)
            for r in range(W.shape[0]):
                mask = (edge_type == r).astype(x.dtype)[:, None]
                m = m + mask * (xj @ W[r])
            m = m * edge_weight[:, None]
            out = jax.ops.segment_sum(m, dst, num_segments=x.shape[0])
            return out + x @ root + bias
        key = jax.random.key(seed)
        ks = jax.random.split(key, 10)
        return {'x': jax.random.normal(ks[0], (N_NODES, F_IN), dtype=jnp.float32), 'edge_index': jax.random.randint(ks[1], (2, N_EDGES), 0, N_NODES, dtype=jnp.int64 if jax.config.jax_enable_x64 else jnp.int32).astype(jnp.int32), 'edge_type': jax.random.randint(ks[2], (N_EDGES,), 0, NUM_RELATIONS).astype(jnp.int32), 'edge_weight': jax.random.uniform(ks[3], (N_EDGES,), dtype=jnp.float32), 'W1': jax.random.normal(ks[4], (NUM_RELATIONS, F_IN, HID), dtype=jnp.float32) * 0.05, 'root1': jax.random.normal(ks[5], (F_IN, HID), dtype=jnp.float32) * 0.05, 'b1': jax.random.normal(ks[6], (HID,), dtype=jnp.float32) * 0.05, 'W2': jax.random.normal(ks[7], (NUM_RELATIONS, HID, EMB), dtype=jnp.float32) * 0.05, 'root2': jax.random.normal(ks[8], (HID, EMB), dtype=jnp.float32) * 0.05, 'b2': jax.random.normal(ks[9], (EMB,), dtype=jnp.float32) * 0.05}
    _L0_gnn_all = _L0_gnn_setup()
    _L0_gnn_in = {k: v for k, v in _L0_gnn_all.items() if k in ('W1', 'root1', 'b1', 'W2', 'root2', 'b2')}
    del _L0_gnn_all

    def _L1_gnn_setup():
        import jax, jax.numpy as jnp
        import numpy as np
        N_NODES = 12500
        N_EDGES = 80000
        DIM = 128
        key = jax.random.key(seed)
        k1, k2, k3, k4, k5 = jax.random.split(key, 5)
        x = jax.random.normal(k1, (N_NODES, DIM), dtype=jnp.float32)
        edge_index = jax.random.randint(k2, (2, N_EDGES), 0, N_NODES, dtype=jnp.int64)
        edge_weight = jax.random.uniform(k3, (N_EDGES,), dtype=jnp.float32)
        W = jax.random.normal(k4, (DIM, DIM), dtype=jnp.float32) * (1.0 / np.sqrt(DIM))
        b = jax.random.normal(k5, (DIM,), dtype=jnp.float32) * 0.01
        return {'x': x, 'edge_index': edge_index, 'edge_weight': edge_weight, 'W': W, 'b': b}
    _L1_gnn_all = _L1_gnn_setup()
    _L1_gnn_in = {k: v for k, v in _L1_gnn_all.items() if k in ('W', 'b')}
    del _L1_gnn_all
    return {'x': x, 'src': src, 'dst': dst, 'edge_type_4': edge_type_4, 'edge_weight': edge_weight, 'L0_gnn_W1': _L0_gnn_in['W1'], 'L0_gnn_root1': _L0_gnn_in['root1'], 'L0_gnn_b1': _L0_gnn_in['b1'], 'L0_gnn_W2': _L0_gnn_in['W2'], 'L0_gnn_root2': _L0_gnn_in['root2'], 'L0_gnn_b2': _L0_gnn_in['b2'], 'L1_gnn_W': _L1_gnn_in['W'], 'L1_gnn_b': _L1_gnn_in['b']}

def reference(x, src, dst, edge_type_4, edge_weight, L0_gnn_W1, L0_gnn_root1, L0_gnn_b1, L0_gnn_W2, L0_gnn_root2, L0_gnn_b2, L1_gnn_W, L1_gnn_b):
    import jax
    import jax.numpy as jnp

    def _L0_gnn_ref(x, edge_index, edge_type, edge_weight, W1, root1, b1, W2, root2, b2):
        import jax, jax.numpy as jnp
        import numpy as np
        NUM_RELATIONS = 4
        N_NODES = 2500
        N_EDGES = 40000
        F_IN = 128
        HID = 128
        EMB = 128

        def _rgcn_conv(x, src, dst, edge_type, edge_weight, W, root, bias):
            xj = x[src]
            m = jnp.zeros((xj.shape[0], W.shape[2]), dtype=x.dtype)
            for r in range(W.shape[0]):
                mask = (edge_type == r).astype(x.dtype)[:, None]
                m = m + mask * (xj @ W[r])
            m = m * edge_weight[:, None]
            out = jax.ops.segment_sum(m, dst, num_segments=x.shape[0])
            return out + x @ root + bias
        src, dst = (edge_index[0], edge_index[1])
        ew = (edge_weight - edge_weight.min()) / (edge_weight.max() - edge_weight.min() + 1e-08)
        h = jax.nn.relu(_rgcn_conv(x, src, dst, edge_type, ew, W1, root1, b1))
        h = _rgcn_conv(h, src, dst, edge_type, ew, W2, root2, b2)
        return h

    def _L1_gnn_ref(x, edge_index, edge_weight, W, b):
        import jax, jax.numpy as jnp
        import numpy as np
        N_NODES = 12500
        N_EDGES = 80000
        DIM = 128
        row, col = (edge_index[0], edge_index[1])
        msgs = edge_weight[:, None] * x[row]
        agg = jax.ops.segment_sum(msgs, col, num_segments=x.shape[0])
        return agg @ W.T + b
    edge_index = jnp.stack([src, dst])
    h = jnp.maximum(_layernorm(x, axis=-1), 0.0)
    x = x + _L0_gnn_ref(h, edge_index, edge_type_4, edge_weight, L0_gnn_W1, L0_gnn_root1, L0_gnn_b1, L0_gnn_W2, L0_gnn_root2, L0_gnn_b2)
    h = jnp.maximum(_layernorm(x, axis=-1), 0.0)
    x = x + _L1_gnn_ref(h, edge_index, edge_weight, L1_gnn_W, L1_gnn_b)
    return x

_drawn_inputs = setup_inputs


def setup_inputs(seed=0):
    import zlib

    import numpy as np

    out = dict(_drawn_inputs(seed))
    spreads = {}
    factors = {'L1_gnn_b': 29.348}
    for name, (base, spread) in spreads.items():
        noise = np.random.default_rng([zlib.crc32(name.encode()), seed]).standard_normal(out[name].shape)
        drawn = base * np.exp(spread * noise) if base else spread * noise
        out[name] = jnp.asarray(drawn.astype(out[name].dtype))
    for name, factor in factors.items():
        out[name] = (out[name] * factor).astype(out[name].dtype)
    return out
```

```python
import concourse.bass as bass
from concourse import mybir
from contextlib import ExitStack

P = 128
CG = 4
GI = 4
NSLOT = CG * GI
W = 48
TB = 4
LN_EPS = 1e-5
RANGE_EPS = 1e-8


def build(nc, x, src, dst, etype, weight, W1, root1, b1, W2, root2, b2, W3, b3, out):
    fp32, bf16, i32 = mybir.dt.float32, mybir.dt.bfloat16, mybir.dt.int32
    ALU, ACT, AX = mybir.AluOpType, mybir.ActivationFunctionType, mybir.AxisListType.X

    N, D = x.shape
    E = src.shape[0]
    R = W1.shape[0]
    NT = -(-N // P)
    NP_ = NT * P
    last_rows = N - (NT - 1) * P
    ACC = max(NP_, N + W)
    C = -(-E // P)
    tail_edges = E - (C - 1) * P
    NG = -(-C // CG)
    NI = -(-NG // GI)
    NB = -(-NT // TB)
    CT = -(-C // P)
    assert D == P and NI == NT and NG <= 512 and R * P <= 512 and R * W <= 512
    assert 4 * CT * P + C <= ACC and NB >= 3 and NT - (NB - 1) * TB in (1, 2, 3, 4)

    MB = -(-CT // 4)
    N_CONST = 6
    REDUCE_MAX = bass.bass_isa.ReduceOp.max
    last_chunks = C - (NI - 1) * NSLOT
    assert NG - (NI - 1) * GI >= 3
    META_INC = 16 * ((CT > 1) + (C - (CT - 1) * P > 1) + 1 + (tail_edges < P))

    table = [nc.dram_tensor(f"table{r}", (NP_, D), fp32, kind="Internal").ap() for r in range(3)]

    def chunks_of(g):
        return min(CG, C - g * CG)

    def tiles_of(b):
        return min(TB, NT - b * TB)

    ctx = ExitStack()
    with ctx:
        def sb(name, shape, dt=fp32):
            return ctx.enter_context(nc.sbuf_tensor(name, shape, dt))

        def ps(name, shape):
            return ctx.enter_context(nc.psum_tensor(name, shape, fp32))

        def sem(name):
            return ctx.enter_context(nc.semaphore(name))

        acc_a, acc_b, acc_c = sb("acc_a", [P, ACC]), sb("acc_b", [P, ACC]), sb("acc_c", [P, ACC])
        src_col = sb("src_col", [P, C], i32)
        key_col = sb("key_col", [P, C])
        type_col = sb("type_col", [P, C], bf16)
        w_col = sb("w_col", [P, C])
        idx = sb("idx", [P, NSLOT], i32)
        rows = sb("rows", [P, NSLOT, D])
        sel = sb("sel", [P, 2, CG, R * W])
        agg = sb("agg", [P, 2, R * W])
        xin = sb("xin", [P, 2, TB * D])
        stage = rows[:, NSLOT - 2 * TB:NSLOT, :].rearrange("p (s t) d -> p s (t d)", s=2)
        hout = sb("hout", [P, 2, TB * D])
        tile_rows = sb("tile_rows", [P, D])
        tile_T = sb("tile_T", [P, P])
        W1s, W2s = sb("W1s", [P, R, D]), sb("W2s", [P, R, D])
        r1s, r2s, W3s, W3T = sb("r1s", [P, D]), sb("r2s", [P, D]), sb("W3s", [P, D]), sb("W3T", [P, D])
        b1s, b2s, b3row, b3bc = sb("b1s", [P, 1]), sb("b2s", [P, 1]), sb("b3row", [1, D]), sb("b3bc", [P, D])
        ident = sb("ident", [P, P])
        row0 = sb("row0", [P, P])
        iota = sb("iota", [P, R * P])
        base_i = sb("base_i", [1, NG], i32)
        stats = sb("stats", [P, 2, TB, 6])
        mv = sb("mv", [P, 2, TB, 2])
        std = sb("std", [P, 2, TB])
        rstd = sb("rstd", [P, 2, TB])
        nmr = sb("nmr", [P, 2, TB])
        ext = sb("ext", [P, 4])
        extg = sb("extg", [P, 4])
        wsc = sb("wsc", [P, 1])
        ewt = sb("ewt", [P, NSLOT])
        eps = sb("eps", [P, 1])
        small = sb("small", [1, 4])
        flag = sb("flag", [1, 1], i32)
        gsel = sel[:, :, :, :].rearrange("p a c w -> p (a c w)")[:, 0:R * P]
        gagg = stage[:, 0, :]
        gtmp = sb("gtmp", [P, 8])

        bank = [ps(f"bank{k}", [P, 512]) for k in range(8)]
        base_ps = bank[0]
        agg_ps, mix_ps, turn_ps, root_ps, dense_ps = bank[0:2], bank[2:4], bank[4], bank[5], bank[6:8]


        s_meta = [sem(f"s_meta{k}") for k in range(4)]
        s_wts = sem("s_wts")
        s_const = sem("s_const")
        s_cast = sem("s_cast")
        s_zero = sem("s_zero")
        s_mT, s_mC = sem("s_mT"), sem("s_mC")
        s_mA = sem("s_mA")
        s_base, s_bcp = sem("s_base"), sem("s_bcp")
        s_d = sem("s_d")
        s_gp = sem("s_gp")
        s_ext, s_extg = sem("s_ext"), sem("s_extg")
        s_flag = sem("s_flag")
        s_w3 = sem("s_w3")
        s_b3, s_w3c = sem("s_b3"), sem("s_w3c")
        s_x = [sem("s_x0"), sem("s_x1")]
        s_tab = [sem("s_tab0"), sem("s_tab1")]
        s_st, s_mv, s_sd, s_rs, s_nm, s_h = (sem(n) for n in ("s_st", "s_mv", "s_sd", "s_rs", "s_nm", "s_h"))
        s_sg, s_tr, s_cx = sem("s_sg"), sem("s_tr"), sem("s_cx")
        s_idx, s_sel, s_agg, s_cp, s_mix, s_acc, s_ew = (
            sem(n) for n in ("s_idx", "s_sel", "s_agg", "s_cp", "s_mix", "s_acc", "s_ew"))
        s_row = [sem(f"s_row{k}") for k in range(NSLOT)]
        s_hold = sem("s_hold")
        s_tl, s_tT, s_tc, s_tm, s_ta = (sem(n) for n in ("s_tl", "s_tT", "s_tc", "s_tm", "s_ta"))
        s_round = sem("s_round")
        s_gi, s_gr, s_gv, s_gs, s_ga, s_gc, s_gm, s_gx, s_gd = (
            sem(n) for n in ("s_gi", "s_gr", "s_gv", "s_gs", "s_ga", "s_gc", "s_gm", "s_gx", "s_gd"))

        def wait(eng, s, v):
            if isinstance(v, int) and v <= 0:
                return
            eng.wait_ge(s, v)

        def hold(eng):
            eng.sem_inc(s_hold)

        def iterations(eng, n, body):
            body(0)
            if n > 2:
                with eng.Fori(1, n - 1) as i:
                    body(i)
            if n > 1:
                body(n - 1)

        def batches(eng, step):
            step(0, 0, TB, 0)
            step(1, 1, TB, 0)
            pairs = (NB - 3) // 2 + 1
            if pairs > 1:
                with eng.Fori(1, pairs) as i:
                    step(i * 2, 0, TB, i)
                    step(i * 2 + 1, 1, TB, i)
            for b in range(2 * pairs, NB):
                step(b, b % 2, tiles_of(b), b // 2)

        def is_last(b):
            return isinstance(b, int) and b == NB - 1

        def node_rows(dram, b, n):
            return dram[bass.ds(b * (TB * P), n * P), :].rearrange("(t p) d -> p t d", p=P)

        def over_groups(eng, group):
            def body(i):
                for q in range(GI):
                    g = i * GI + q
                    if not isinstance(g, int):
                        group(i, g, q, CG)
                    elif g < NG:
                        group(i, g, q, chunks_of(g))
            iterations(eng, NI, body)

        block = ctx.enter_context(nc.Block())

        def load_x(eng, b, s, n, free, freed):
            wait(eng, free, freed)
            if is_last(b) and last_rows < P:
                if n > 1:
                    eng.dma_start(xin[:, s, 0:(n - 1) * D].rearrange("p (t d) -> p t d", d=D),
                                  node_rows(x, b, n - 1)).then_inc(s_x[s], 16)
                eng.dma_start(xin[0:last_rows, s, (n - 1) * D:n * D], x[(NT - 1) * P:N, :]).then_inc(s_x[s], 16)
            else:
                eng.dma_start(xin[:, s, 0:n * D].rearrange("p (t d) -> p t d", d=D),
                              node_rows(x, b, n)).then_inc(s_x[s], 16)

        def x_loads(b):
            return 2 if is_last(b) and last_rows < P and tiles_of(b) > 1 else 1

        per_slot = [(NB + 1) // 2, NB // 2]
        x_per_phase = [16 * (per_slot[k] + (1 if (NB - 1) % 2 == k and x_loads(NB - 1) == 2 else 0)) for k in (0, 1)]
        out_per_phase = x_per_phase

        def x_wait(phase, b, s, h):
            return h * 16 + (phase * x_per_phase[s] + 16 * x_loads(b))

        def row_base(r, slot):
            return 16 * r * (NI - 1 + (slot < last_chunks))

        @block.sync
        def _(eng):
            def out_rows(dram, b, s, n, done, done_v, exact=False):
                wait(eng, done, done_v)
                if exact and is_last(b) and last_rows < P:
                    if n > 1:
                        eng.dma_start(node_rows(dram, b, n - 1),
                                      hout[:, s, 0:(n - 1) * D].rearrange("p (t d) -> p t d", d=D)).then_inc(s_tab[s], 16)
                    eng.dma_start(dram[(NT - 1) * P:N, :], hout[0:last_rows, s, (n - 1) * D:n * D]).then_inc(s_tab[s], 16)
                else:
                    eng.dma_start(node_rows(dram, b, n),
                                  hout[:, s, 0:n * D].rearrange("p (t d) -> p t d", d=D)).then_inc(s_tab[s], 16)

            def p0(b, s, n, h):
                load_x(eng, b, s, n, s_h, b - 1)
                if not (isinstance(b, int) and b < 2):
                    out_rows(table[0], b - 2, s, TB, s_h, b - 1)
            batches(eng, p0)
            for b in (NB - 2, NB - 1):
                out_rows(table[0], b, b % 2, tiles_of(b), s_h, b + 1)

            def tile_load(i):
                wait(eng, s_tT, i)
                eng.dma_start(tile_rows[:, :], table[0][bass.ds(i * P, P), :]).then_inc(s_tl, 16)
            for k in (0, 1):
                eng.wait_ge(s_tab[k], 16 * per_slot[k])
            iterations(eng, NT, tile_load)

            def e1(b, s, n, h):
                out_rows(table[1], b, s, n, s_cx, b + 1)
            batches(eng, e1)

            def e2(b, s, n, h):
                load_x(eng, b, s, n, s_cx, b + (NB - 1))
                if not (isinstance(b, int) and b < 2):
                    out_rows(table[2], b - 2, s, TB, s_h, b + (NB - 1))
            batches(eng, e2)
            for b in (NB - 2, NB - 1):
                out_rows(table[2], b, b % 2, tiles_of(b), s_h, b + NB + 1)

            def e3(b, s, n, h):
                out_rows(out, b, s, n, s_cx, b + (2 * NB + 1), exact=True)
            batches(eng, e3)
            for k in (0, 1):
                eng.wait_ge(s_tab[k], 3 * 16 * per_slot[k] + out_per_phase[k])

        @block.gpsimd
        def _(eng):
            def const(ins):
                ins.then_inc(s_const, 1)
            const(eng.memset(ident[:, :], 0.0))
            const(eng.memset(row0[:, :], 0.0))
            const(eng.memset(eps[:, :], LN_EPS))
            const(eng.iota(iota[:, :], [[1, R * P]], base=0, channel_multiplier=0,
                           allow_small_or_imprecise_dtypes=True))
            eng.wait_ge(s_const, 2)
            const(eng.affine_select(out=ident[:, :], in_=ident[:, :], compare_op=ALU.not_equal, fill=1.0,
                                    base=0, pattern=[[-1, P]], channel_multiplier=1))
            const(eng.memset(row0[0:1, :], 1.0))
            for a in (0, 1, 2):
                eng.wait_ge(s_meta[a], META_INC)
                full = (CT - 1) * P
                lo = a * CT * P
                if CT > 1:
                    eng.tensor_copy(acc_a[:, lo:lo + full], acc_a[:, lo:lo + full].bitcast(i32))
                last = C - (CT - 1) * P
                eng.tensor_copy(acc_a[0:last, lo + full:lo + CT * P],
                                acc_a[0:last, lo + full:lo + CT * P].bitcast(i32)).then_inc(s_cast, 1)
            eng.memset(acc_b[:, :], 0.0).then_inc(s_zero, 1)
            eng.memset(acc_c[:, :], 0.0).then_inc(s_zero, 1)
            eng.wait_ge(s_ext, 1)
            eng.partition_all_reduce(extg[:, :], ext[:, :], P, REDUCE_MAX).then_inc(s_extg, 1)

            eng.wait_ge(s_flag, 1)
            narrow = eng.value_load(flag[0:1, 0:1], min_val=0, max_val=1)

            def fast(r):
                def group(i, g, q, n):
                    wait(eng, s_idx, g + (r * NG + 1))
                    hold(eng)
                    for k in range(q * CG, q * CG + n):
                        eng.indirect_dma_start(
                            out=rows[:, k, :], out_offset=None, in_=table[r][:, :],
                            in_offset=bass.IndirectOffsetOnAxis(ap=idx[:, k:k + 1], axis=0)).then_inc(s_row[k], 16)
                over_groups(eng, group)

            def general(r):
                def chunk(c):
                    eng.wait_ge(s_gi, c + (r * C + 1))
                    hold(eng)
                    eng.indirect_dma_start(
                        out=rows[:, 0, :], out_offset=None, in_=table[r][:, :],
                        in_offset=bass.IndirectOffsetOnAxis(ap=idx[:, 0:1], axis=0)).then_inc(s_gr, 16)
                with eng.Fori(0, C) as c:
                    chunk(c)

            for r in range(3):
                for k in (0, 1):
                    eng.wait_ge(s_tab[k], 16 * per_slot[k] * (r + 1))
                with eng.If(narrow == 1):
                    fast(r)
                with eng.Else():
                    general(r)
                if r == 0:
                    eng.wait_ge(s_round, 1)
                    eng.memset(acc_a[:, :], 0.0).then_inc(s_zero, 1)

        @block.scalar
        def _(eng):
            for a, arr in enumerate((src, dst, etype, weight)):
                to = acc_a[:, a * CT * P:(a + 1) * CT * P]
                if arr is not weight:
                    to = to.bitcast(i32)
                full = (CT - 1) * P
                if CT > 1:
                    eng.dma_start(to[:, 0:full].rearrange("p (t e) -> p t e", e=P),
                                  arr[0:full * P].rearrange("(t p e) -> p t e", p=P, e=P)).then_inc(s_meta[a], 16)
                rest = C - full - 1
                if rest:
                    eng.dma_start(to[0:rest, full:full + P],
                                  arr[full * P:(C - 1) * P].rearrange("(p e) -> p e", e=P)).then_inc(s_meta[a], 16)
                eng.dma_start(to[rest:rest + 1, full:full + tail_edges],
                              arr[(C - 1) * P:E].rearrange("(p e) -> p e", p=1)).then_inc(s_meta[a], 16)
                if tail_edges < P:
                    eng.dma_start(to[rest:rest + 1, full + tail_edges:full + P],
                                  arr[E - (P - tail_edges):E].rearrange("(p e) -> p e", p=1)).then_inc(s_meta[a], 16)
            for to, fr in ((W1s[:, :, :], W1.rearrange("r f o -> f r o")), (W2s[:, :, :], W2.rearrange("r f o -> f r o")),
                           (r1s[:, :], root1), (r2s[:, :], root2), (W3s[:, :], W3),
                           (b1s[:, :], b1.rearrange("(p a) -> p a", a=1)), (b2s[:, :], b2.rearrange("(p a) -> p a", a=1)),
                           (b3row[:, :], b3.rearrange("(a n) -> a n", a=1))):
                eng.dma_start(to, fr).then_inc(s_wts, 16)

            def meta_copy(n):
                a, t = divmod(n, MB)
                wd = min(4 * P, C - t * 4 * P)
                eng.wait_ge(s_mT, n + 1)
                o = (type_col if a == 2 else w_col)[:, t * 4 * P:t * 4 * P + wd]
                eng.activation(o, bank[4 + n % 4][:, 0:wd], ACT.Copy, scale=1.0).then_inc(s_mA, 1)

            def norm(base, done_base, b, s, n, h, src_of):
                wait(eng, s_nm, b + (base + 1))
                wait(eng, s_tab[s], 16 * h + 16 * per_slot[s] * done_base)
                for t in range(n):
                    ins = eng.activation(hout[:, s, t * D:(t + 1) * D], src_of(b, s, t), ACT.Relu,
                                         bias=nmr[:, s, t:t + 1], scale=rstd[:, s, t:t + 1])
                ins.then_inc(s_h, 1)

            def root_of_var(base, b, s, n):
                wait(eng, s_mv, b + (base + 1))
                wait(eng, s_nm, b + (base - 1))
                eng.activation(std[:, s, 0:n], mv[:, s, 0:n, 1], ACT.Sqrt, bias=eps[:, 0:1]).then_inc(s_sd, 1)

            eng.wait_ge(s_const, N_CONST)

            def p0_norm(b, s, n, h):
                norm(0, 0, b, s, n, h, lambda b, s, t: xin[:, s, t * D:(t + 1) * D])

            def p0(b, s, n, h):
                root_of_var(0, b, s, n)
                if not (isinstance(b, int) and b == 0):
                    p0_norm(b - 1, 1 - s, TB, h - (1 - s))
            batches(eng, p0)
            p0_norm(NB - 1, (NB - 1) % 2, tiles_of(NB - 1), (NB - 1) // 2)
            for n in range(2 * MB, 4 * MB):
                meta_copy(n)

            eng.wait_ge(s_flag, 1)
            narrow = eng.value_load(flag[0:1, 0:1], min_val=0, max_val=1)

            def tile_step(r, i):
                if r == 0:
                    wait(eng, s_tT, i + 1)
                    wait(eng, s_tm, i)
                    eng.activation(tile_T[:, :], turn_ps[:, 0:P], ACT.Copy).then_inc(s_tc, 1)
                else:
                    wait(eng, s_tm, i + NT)
                    eng.activation(tile_T[:, :], acc_b[:, bass.ds(i * P, P)], ACT.Relu).then_inc(s_tc, 1)

            def fast(r):
                def group(i, g, q, n):
                    if q == 0:
                        tile_step(r, i)
                    wait(eng, s_agg, g + (r * NG + 1))
                    wait(eng, s_mix, g + (r * NG - 1))
                    eng.activation(agg[:, q % 2, :], agg_ps[q % 2][:, 0:R * W], ACT.Copy).then_inc(s_cp, 1)
                over_groups(eng, group)

            def general(r):
                def tile(i):
                    tile_step(r, i)
                iterations(eng, NT, tile)

                with eng.Fori(0, C) as c:
                    with eng.Fori(0, NT) as v:
                        eng.wait_ge(s_ga, c * NT + v + (r * C * NT + 1))
                        eng.activation(gagg[:, 0:R * P], agg_ps[0][:, 0:R * P], ACT.Copy).then_inc(s_gc, 1)

            with eng.If(narrow == 1):
                fast(0)
            with eng.Else():
                general(0)

            eng.wait_ge(s_round, 1)

            def e1(b, s, n, h):
                wait(eng, s_tr, b - 1)
                eng.activation(stage[:, s, 0:n * P], acc_b[:, bass.ds(b * (TB * P), n * P)], ACT.Relu).then_inc(s_sg, 1)
            batches(eng, e1)

            with eng.If(narrow == 1):
                fast(1)
            with eng.Else():
                general(1)

            eng.wait_ge(s_round, 2)

            def e2_stage(b, s, n, h):
                wait(eng, s_tr, b + (NB - 1))
                eng.activation(stage[:, s, 0:n * P], acc_c[:, bass.ds(b * (TB * P), n * P)], ACT.Copy).then_inc(s_sg, 1)

            def e2_norm(b, s, n, h):
                norm(NB, 2, b, s, n, h, lambda b, s, t: acc_b[:, bass.ds(b * (TB * P) + t * P, P)])

            def e2(b, s, n, h):
                e2_stage(b, s, n, h)
                if not (isinstance(b, int) and b == 0):
                    root_of_var(NB, b - 1, 1 - s, TB)
                if not (isinstance(b, int) and b < 2):
                    e2_norm(b - 2, s, TB, h - 1)
            batches(eng, e2)
            root_of_var(NB, NB - 1, (NB - 1) % 2, tiles_of(NB - 1))
            e2_norm(NB - 2, NB % 2, TB, (NB - 2) // 2)
            e2_norm(NB - 1, (NB - 1) % 2, tiles_of(NB - 1), (NB - 1) // 2)

            eng.wait_ge(s_round, 3)

            def e3(b, s, n, h):
                wait(eng, s_tr, b + (2 * NB - 1))
                eng.activation(stage[:, s, 0:n * P], acc_a[:, bass.ds(b * (TB * P), n * P)], ACT.Copy).then_inc(s_sg, 1)
            batches(eng, e3)

        @block.tensor
        def _(eng):
            eng.wait_ge(s_const, N_CONST)
            for n in range(4 * MB):
                a, t4 = divmod(n, MB)
                if n == 2 * MB:
                    eng.wait_ge(s_mC, 2 * MB)
                    eng.matmul(base_ps[:, 0:NG], row0[:, :], key_col[:, 0:C:CG], start=True, stop=True).then_inc(s_base, 1)
                if t4 == 0:
                    if a < 3:
                        eng.wait_ge(s_cast, a + 1)
                    else:
                        eng.wait_ge(s_meta[3], META_INC)
                if n >= 4:
                    m = n - 4
                    wait(eng, s_mC, min(m + 1, 2 * MB))
                    wait(eng, s_mA, m + 1 - 2 * MB)
                for t in range(4 * t4, min(4 * t4 + 4, CT)):
                    k = min(P, C - t * P)
                    lo = a * CT * P + t * P
                    ins = eng.transpose(bank[4 + n % 4][:, (t % 4) * P:(t % 4) * P + k], acc_a[0:k, lo:lo + P],
                                        ident[0:k, 0:k])
                ins.then_inc(s_mT, 1)
            eng.wait_ge(s_wts, 16 * 8)
            eng.transpose(agg_ps[1][:, 0:P], W3s[:, :], ident[:, :])
            eng.matmul(agg_ps[1][:, P:2 * P], row0[0:1, :], b3row[0:1, :], start=True, stop=True).then_inc(s_w3, 1)

            eng.wait_ge(s_flag, 1)
            narrow = eng.value_load(flag[0:1, 0:1], min_val=0, max_val=1)
            eng.wait_ge(s_w3c, 2)

            def turn_tile(i):
                wait(eng, s_tl, (i + 1) * 16)
                wait(eng, s_tc, i)
                eng.transpose(turn_ps[:, 0:P], tile_rows[:, :], ident[:, :]).then_inc(s_tT, 1)

            def root_tile(r, i):
                wait(eng, s_tc, i + (r * NT + 1))
                wait(eng, s_ta, i + r * NT)
                eng.matmul(root_ps[:, 0:P], (r1s if r == 0 else r2s)[:, :], tile_T[:, :],
                           start=True, stop=True).then_inc(s_tm, 1)

            def fast(r):
                wr = (W1s, W2s, None)[r]
                width = R * W if r < 2 else W

                def mix(g, q):
                    wait(eng, s_cp, g + (r * NG + 1))
                    wait(eng, s_acc, g + (r * NG - 1))
                    for k in range(R):
                        ins = eng.matmul(mix_ps[q % 2][:, 0:W], wr[:, k, :], agg[:, q % 2, k * W:(k + 1) * W],
                                         start=(k == 0), stop=(k == R - 1))
                    ins.then_inc(s_mix, 1)

                def group(i, g, q, n):
                    wait(eng, s_sel, g + (r * NG + 1))
                    if r < 2:
                        wait(eng, s_cp, g + (r * NG - 1) if not (isinstance(g, int) and g < 2) else 0)
                    else:
                        wait(eng, s_acc, g + (r * NG - 1) if not (isinstance(g, int) and g < 2) else 0)
                    for k in range(n):
                        slot = q * CG + k
                        wait(eng, s_row[slot], i * 16 + (row_base(r, slot) + 16))
                        ins = eng.matmul(agg_ps[q % 2][:, 0:width], rows[:, slot, :], sel[:, q % 2, k, 0:width],
                                         start=(k == 0), stop=(k == n - 1))
                    ins.then_inc(s_agg, 1)
                    if r < 2:
                        if not (isinstance(g, int) and g == 0):
                            mix(g - 1, q - 1 + GI)
                        if q == 0 and r == 0:
                            turn_tile(i)
                        if q == 1:
                            root_tile(r, i)
                over_groups(eng, group)
                if r < 2:
                    mix(NG - 1, (NG - 1) % GI)

            def general(r):
                if r < 2:
                    def tile(i):
                        if r == 0:
                            turn_tile(i)
                        root_tile(r, i)
                    iterations(eng, NT, tile)
                with eng.Fori(0, C) as c:
                    eng.wait_ge(s_gr, (c + (r * C + 1)) * 16)
                    eng.sem_inc(s_gd)
                    with eng.Fori(0, NT) as v:
                        ev = c * NT + v + r * C * NT
                        eng.wait_ge(s_gs, ev + 1)
                        wd = R * P if r < 2 else P
                        eng.matmul(agg_ps[0][:, 0:wd], rows[:, 0, :], gsel[:, 0:wd], start=True, stop=True).then_inc(s_ga, 1)
                        if r < 2:
                            eng.wait_ge(s_gc, ev + 1)
                            for k in range(R):
                                ins = eng.matmul(mix_ps[0][:, 0:P], (W1s, W2s)[r][:, k, :], gagg[:, k * P:(k + 1) * P],
                                                 start=(k == 0), stop=(k == R - 1))
                            ins.then_inc(s_gm, 1)

            def turn(base, b, s, n):
                wait(eng, s_sg, b + (base + 1))
                wait(eng, s_cx, b + (base - 1))
                for t in range(n):
                    ins = eng.transpose(dense_ps[s][:, t * P:(t + 1) * P], stage[:, s, t * P:(t + 1) * P], ident[:, :])
                ins.then_inc(s_tr, 1)

            with eng.If(narrow == 1):
                fast(0)
            with eng.Else():
                general(0)
            batches(eng, lambda b, s, n, h: turn(0, b, s, n))
            with eng.If(narrow == 1):
                fast(1)
            with eng.Else():
                general(1)
            batches(eng, lambda b, s, n, h: turn(NB, b, s, n))
            with eng.If(narrow == 1):
                fast(2)
            with eng.Else():
                general(2)

            def e3(b, s, n, h):
                wait(eng, s_sg, b + (2 * NB + 1))
                wait(eng, s_cx, b + (2 * NB - 1))
                for t in range(n):
                    ins = eng.matmul(dense_ps[s][:, t * P:(t + 1) * P], stage[:, s, t * P:(t + 1) * P], W3T[:, :],
                                     start=True, stop=True)
                ins.then_inc(s_tr, 1)
            batches(eng, e3)

        @block.vector
        def _(eng):
            steps = {s_d: 0, s_gp: 0}

            def link(ins, s=s_d):
                steps[s] += 1
                ins.then_inc(s, 1)
                eng.wait_ge(s, steps[s])

            def statistics(base, b, s, n, src_of):
                wait(eng, s_mv, b + (base - 1))
                hold(eng)
                for t in range(n):
                    ins = eng.bn_stats(stats[:, s, t, :], src_of(b, s, t))
                ins.then_inc(s_st, 1)
                wait(eng, s_st, b + (base + 1))
                wait(eng, s_nm, b + (base - 1))
                hold(eng)
                for t in range(n):
                    ins = eng.bn_aggr(mv[:, s, t, :], stats[:, s, t, :])
                ins.then_inc(s_mv, 1)

            def scale_shift(base, b, s, n):
                wait(eng, s_sd, b + (base + 1))
                wait(eng, s_h, b + (base - 1))
                eng.reciprocal(rstd[:, s, 0:n], std[:, s, 0:n]).then_inc(s_rs, 1)
                wait(eng, s_rs, b + (base + 1))
                eng.scalar_tensor_tensor(out=nmr[:, s, 0:n], in0=mv[:, s, 0:n, 0], scalar=-1.0, in1=rstd[:, s, 0:n],
                                         op0=ALU.mult, op1=ALU.mult).then_inc(s_nm, 1)

            def meta_copy(n):
                a, t = divmod(n, MB)
                wd = min(4 * P, C - t * 4 * P)
                eng.wait_ge(s_mT, n + 1)
                o = (src_col if a == 0 else key_col)[:, t * 4 * P:t * 4 * P + wd]
                eng.tensor_copy(o, bank[4 + n % 4][:, 0:wd]).then_inc(s_mC, 1)

            for n in range(2 * MB):
                meta_copy(n)
            rel = acc_a[:, 4 * CT * P:4 * CT * P + C]
            eng.wait_ge(s_base, 1)
            gfull = C // CG
            eng.tensor_copy(base_i[0:1, :], base_ps[0:1, 0:NG]).then_inc(s_bcp, 1)
            eng.wait_ge(s_mC, 2 * MB)
            link(eng.tensor_tensor(
                rel[:, 0:gfull * CG].rearrange("p (g j) -> p g j", j=CG),
                key_col[:, 0:gfull * CG].rearrange("p (g j) -> p g j", j=CG),
                base_ps[:, 0:gfull].unsqueeze(2).to_broadcast([P, gfull, CG]), ALU.subtract))
            if C > gfull * CG:
                link(eng.tensor_scalar(rel[:, gfull * CG:C], key_col[:, gfull * CG:C], base_ps[:, gfull:gfull + 1],
                                       None, ALU.subtract))
            eng.tensor_reduce(ext[:, 0:1], rel, axis=AX, op=ALU.max)
            link(eng.tensor_reduce(ext[:, 1:2], rel, axis=AX, op=ALU.min))

            def p0(b, s, n, h):
                wait(eng, s_x[s], x_wait(0, b, s, h))
                statistics(0, b, s, n, lambda b, s, t: xin[:, s, t * D:(t + 1) * D])
                if not (isinstance(b, int) and b == 0):
                    scale_shift(0, b - 1, 1 - s, TB)
            batches(eng, p0)
            scale_shift(0, NB - 1, (NB - 1) % 2, tiles_of(NB - 1))

            eng.wait_ge(s_mA, 2 * MB)
            eng.tensor_reduce(ext[:, 2:3], w_col[:, :], axis=AX, op=ALU.max)
            link(eng.tensor_reduce(ext[:, 3:4], w_col[:, :], axis=AX, op=ALU.min))
            link(eng.tensor_scalar(ext[:, 1:2], ext[:, 1:2], -1.0, None, ALU.mult))
            eng.tensor_scalar(ext[:, 3:4], ext[:, 3:4], -1.0, None, ALU.mult).then_inc(s_ext, 1)
            eng.wait_ge(s_extg, 1)
            link(eng.tensor_tensor(wsc[:, :], extg[:, 2:3], extg[:, 3:4], ALU.add))
            link(eng.tensor_scalar(wsc[:, :], wsc[:, :], RANGE_EPS, None, ALU.add))
            link(eng.reciprocal(wsc[:, :], wsc[:, :]))
            link(eng.tensor_scalar(small[:, 0:1], extg[0:1, 0:1], float(W), None, ALU.is_lt))
            link(eng.tensor_scalar(small[:, 1:2], extg[0:1, 1:2], 0.0, None, ALU.is_le))
            link(eng.tensor_tensor(small[:, 2:3], small[:, 0:1], small[:, 1:2], ALU.mult))
            eng.wait_ge(s_bcp, 1)
            eng.tensor_copy(flag[:, :], small[:, 2:3]).then_inc(s_flag, 1)
            eng.wait_ge(s_w3, 1)
            eng.tensor_copy(W3T[:, :], agg_ps[1][:, 0:P]).then_inc(s_w3c, 1)
            eng.tensor_copy(b3bc[:, :], agg_ps[1][:, P:2 * P]).then_inc(s_w3c, 1)
            eng.wait_ge(s_w3c, 2)
            eng.wait_ge(s_flag, 1)
            narrow = eng.value_load(flag[0:1, 0:1], min_val=0, max_val=1)

            def no_pads(s):
                if tail_edges < P:
                    link(eng.memset(key_col[tail_edges:P, C - 1:C], -1.0), s)

            acc_of = (acc_b, acc_c, acc_a)
            bias_of = (b1s, b2s)

            def tile_step(r, i, after):
                if r < 2:
                    wait(eng, s_tm, i + (r * NT + 1))
                    after()
                    a = acc_of[r][:, bass.ds(i * P, P)]
                    eng.scalar_tensor_tensor(out=a, in0=root_ps[:, 0:P], scalar=bias_of[r][:, 0:1], in1=a,
                                             op0=ALU.add, op1=ALU.add).then_inc(s_ta, 1)
                else:
                    a = acc_b[:, bass.ds(i * P, P)]
                    eng.tensor_tensor(a, a, b3bc[:, :], ALU.add).then_inc(s_ta, 1)

            def fast(r):
                width = R * W if r < 2 else W
                T = r * NG

                def scale_weights(c, k, m):
                    eng.tensor_scalar(ewt[:, k:k + m], w_col[:, bass.ds(c, m)], extg[:, 3:4], wsc[:, 0:1],
                                      ALU.add, ALU.mult).then_inc(s_ew, 1)
                for q in range(GI):
                    if r < 2:
                        scale_weights(q * CG, q * CG, CG)
                    eng.tensor_copy(idx[:, q * CG:(q + 1) * CG], src_col[:, q * CG:(q + 1) * CG]).then_inc(s_idx, 1)
                if r == 0:
                    link(eng.scalar_tensor_tensor(out=key_col[:, :], in0=type_col[:, :], scalar=float(W), in1=rel,
                                                  op0=ALU.mult, op1=ALU.add))
                    no_pads(s_d)
                elif r == 2:
                    link(eng.scalar_tensor_tensor(out=key_col[:, :], in0=type_col[:, :], scalar=-float(W), in1=key_col[:, :],
                                                  op0=ALU.mult, op1=ALU.add))
                    no_pads(s_d)

                def add_window(g, q):
                    base = eng.value_load(base_i[0:1, bass.ds(g, 1)], min_val=0, max_val=N - 1)
                    fr = (mix_ps if r < 2 else agg_ps)[q % 2]
                    wait(eng, s_mix if r < 2 else s_agg, g + (T + 1))
                    wait(eng, s_acc, g + T)
                    a = acc_of[r][:, bass.ds(base, W)]
                    eng.tensor_tensor(a, a, fr[:, 0:W], ALU.add).then_inc(s_acc, 1)

                def group(i, g, q, n):
                    early = isinstance(g, int) and g < 2
                    if not early:
                        wait(eng, s_agg, g + (T - 1))
                        if not (isinstance(g, int) and g + 2 >= NG):
                            m = chunks_of(g + 2) if isinstance(g, int) else CG
                            k = ((q + 2) % GI) * CG
                            eng.tensor_copy(idx[:, k:k + m], src_col[:, bass.ds(g * CG + 2 * CG, m)]).then_inc(s_idx, 1)
                            if r < 2:
                                scale_weights(g * CG + 2 * CG, k, m)
                    if r < 2:
                        wait(eng, s_ew, g + (T + 1))
                    for k in range(n):
                        c = q * CG + k
                        wt = ewt[:, c:c + 1] if r < 2 else w_col[:, bass.ds(i * NSLOT + c, 1)]
                        ins = eng.tensor_scalar(sel[:, q % 2, k, 0:width], iota[:, 0:width],
                                                key_col[:, bass.ds(i * NSLOT + c, 1)], wt, ALU.is_equal, ALU.mult)
                    ins.then_inc(s_sel, 1)
                    if not early:
                        add_window(g - 2, q)
                    if q == 2:
                        tile_step(r, i, lambda: wait(eng, s_acc, g + (T - 1)))
                        wait(eng, s_ta, i + (r * NT + 1))
                eng.wait_ge(s_zero, (1, 2, 3)[r])
                over_groups(eng, group)
                add_window(NG - 2, (NG - 2) % GI)
                add_window(NG - 1, (NG - 1) % GI)
                eng.wait_ge(s_acc, T + NG)

            def round_(r):
                with eng.If(narrow == 1):
                    fast(r)
                with eng.Else():
                    general_path(r)
                eng.sem_inc(s_round)

            def general_path(r):
                wd = R * P if r < 2 else P
                T = r * C * NT
                eng.wait_ge(s_zero, (1, 2, 3)[r])
                if r == 0:
                    no_pads(s_gp)
                if r == 2:
                    eng.wait_ge(s_h, 2 * NB)

                def tile(i):
                    tile_step(r, i, lambda: None)
                iterations(eng, NT, tile)
                eng.wait_ge(s_ta, (r + 1) * NT)
                V = s_gv
                v_per = 8
                with eng.Fori(0, C) as c:
                    key, start, v0, ok, ty, wt = (gtmp[:, k:k + 1] for k in range(6))
                    cb = (c + r * C) * (NT * v_per + 3)
                    eng.tensor_copy(idx[:, 0:1], src_col[:, bass.ds(c, 1)]).then_inc(s_gi, 1)
                    eng.memset(start, 0.0).then_inc(V, 1)
                    eng.tensor_scalar(ty, type_col[:, bass.ds(c, 1)], float(P), 1.0, ALU.mult, ALU.add).then_inc(V, 1)
                    if r < 2:
                        eng.tensor_scalar(wt, w_col[:, bass.ds(c, 1)], extg[:, 3:4], wsc[:, 0:1], ALU.add, ALU.mult).then_inc(V, 1)
                    else:
                        eng.tensor_copy(wt, w_col[:, bass.ds(c, 1)]).then_inc(V, 1)
                    with eng.Fori(0, NT) as v:
                        ev = c * NT + v + T
                        vb = cb + v * v_per + 3
                        eng.wait_ge(V, vb)
                        eng.tensor_tensor(v0, key_col[:, bass.ds(c, 1)], start, ALU.subtract).then_inc(V, 1)
                        eng.wait_ge(V, vb + 1)
                        eng.tensor_scalar(ok, v0, 0.0, None, ALU.is_ge).then_inc(V, 1)
                        eng.tensor_scalar(key, v0, float(P), None, ALU.is_lt).then_inc(V, 1)
                        eng.wait_ge(V, vb + 3)
                        eng.tensor_tensor(ok, ok, key, ALU.mult).then_inc(V, 1)
                        if r < 2:
                            eng.tensor_tensor(v0, v0, ty, ALU.add).then_inc(V, 1)
                        else:
                            eng.tensor_scalar(v0, v0, 1.0, None, ALU.add).then_inc(V, 1)
                        eng.wait_ge(V, vb + 5)
                        eng.tensor_tensor(v0, v0, ok, ALU.mult).then_inc(V, 1)
                        eng.tensor_scalar(start, start, float(P), None, ALU.add).then_inc(V, 1)
                        eng.wait_ge(V, vb + 7)
                        eng.tensor_scalar(v0, v0, -1.0, None, ALU.add).then_inc(V, 1)
                        eng.wait_ge(V, vb + 8)
                        eng.tensor_scalar(gsel[:, 0:wd], iota[:, 0:wd], v0, wt, ALU.is_equal, ALU.mult).then_inc(s_gs, 1)
                        fr = (mix_ps if r < 2 else agg_ps)[0]
                        if r < 2:
                            eng.wait_ge(s_gm, ev + 1)
                        else:
                            eng.wait_ge(s_ga, ev + 1)
                        a = acc_of[r][:, bass.ds(v * P, P)]
                        eng.tensor_tensor(a, a, fr[:, 0:P], ALU.add).then_inc(s_gx, 1)
                        eng.wait_ge(s_gx, ev + 1)

            round_(0)

            def e1(b, s, n, h):
                wait(eng, s_tr, b + 1)
                wait(eng, s_tab[s], h * 16 + 16 * per_slot[s])
                eng.tensor_copy(hout[:, s, 0:n * D], dense_ps[s][:, 0:n * P]).then_inc(s_cx, 1)
            batches(eng, e1)
            round_(1)

            def e2(b, s, n, h):
                wait(eng, s_x[s], x_wait(1, b, s, h))
                wait(eng, s_tr, b + (NB + 1))
                eng.tensor_tensor(acc_b[:, bass.ds(b * (TB * P), n * P)], xin[:, s, 0:n * D], dense_ps[s][:, 0:n * P],
                                  ALU.add).then_inc(s_cx, 1)
                wait(eng, s_cx, b + (NB + 1))
                statistics(NB, b, s, n, lambda b, s, t: acc_b[:, bass.ds(b * (TB * P) + t * P, P)])
                if not (isinstance(b, int) and b == 0):
                    scale_shift(NB, b - 1, 1 - s, TB)
            batches(eng, e2)
            scale_shift(NB, NB - 1, (NB - 1) % 2, tiles_of(NB - 1))
            round_(2)

            def e3(b, s, n, h):
                wait(eng, s_tr, b + (2 * NB + 1))
                wait(eng, s_tab[s], 16 * h + 3 * 16 * per_slot[s])
                eng.tensor_tensor(hout[:, s, 0:n * D], acc_b[:, bass.ds(b * (TB * P), n * P)], dense_ps[s][:, 0:n * P],
                                  ALU.add).then_inc(s_cx, 1)
            batches(eng, e3)


_INS = ['x', 'src', 'dst', 'edge_type_4', 'edge_weight', 'L0_gnn_W1', 'L0_gnn_root1', 'L0_gnn_b1', 'L0_gnn_W2',
        'L0_gnn_root2', 'L0_gnn_b2', 'L1_gnn_W', 'L1_gnn_b']


def kernel(**inputs):
    import numpy as _np
    import concourse.bacc as _bacc
    from concourse import mybir as _mybir
    from concourse.bass_utils import run_bass_kernel_spmd as _run

    nc = _bacc.Bacc("TRN2", target_bir_lowering=False, num_devices=1)
    arrays, args = {}, []
    for name in _INS:
        a = _np.ascontiguousarray(inputs[name])
        arrays[f"in_{name}_dram"] = a
        args.append(nc.dram_tensor(f"in_{name}_dram", a.shape, _mybir.dt.from_np(a.dtype), kind="ExternalInput").ap())
    x = inputs['x']
    args.append(nc.dram_tensor("out_0_dram", tuple(x.shape), _mybir.dt.float32, kind="ExternalOutput").ap())
    build(nc, *args)
    r = _run(nc, [arrays], core_ids=[0])
    return r.results[0]["out_0_dram"]
```

```python
import concourse.bass as bass
from concourse import mybir
from contextlib import ExitStack

P = 128
CG = 4
GI = 4
NSLOT = CG * GI
W = 48
TB = 4
BS = 4
TS = 14
SS = 2
LN_EPS = 1e-5
RANGE_EPS = 1e-8


def build(nc, x, src, dst, etype, weight, W1, root1, b1, W2, root2, b2, W3, b3, out):
    fp32, bf16, i32 = mybir.dt.float32, mybir.dt.bfloat16, mybir.dt.int32
    ALU, ACT, AX = mybir.AluOpType, mybir.ActivationFunctionType, mybir.AxisListType.X
    REDUCE_MAX = bass.bass_isa.ReduceOp.max

    N, D = x.shape
    E = src.shape[0]
    R = W1.shape[0]
    NT = -(-N // P)
    last_rows = N - (NT - 1) * P
    ACC = max(NT * P, N + W)
    C = -(-E // P)
    tail_edges = E - (C - 1) * P
    NG = -(-C // CG)
    NI = -(-NG // GI)
    last_chunks = C - (NI - 1) * NSLOT
    NB = -(-NT // TB)
    NS = -(-NT // TS)
    CT = -(-C // P)
    MB = -(-CT // 4)
    STAT = max(TS * SS, TB * BS)
    LIST_LOADS = (CT > 1) + (C - (CT - 1) * P > 1) + 1 + (tail_edges < P)
    split_last = last_rows < P
    assert D == P and NI == NT and NG - (NI - 1) * GI >= 3 and NG <= 512
    assert R * P <= 512 and 4 * CT * P + C <= ACC and NB > BS

    table = [nc.dram_tensor(f"table{r}", (NT * P, D), fp32, kind="Internal").ap() for r in range(3)]

    ctx = ExitStack()
    with ctx:
        def sb(name, shape, dt=fp32):
            return ctx.enter_context(nc.sbuf_tensor(name, shape, dt))

        def sem(name):
            return ctx.enter_context(nc.semaphore(name))

        node = sb("node", [P, NT * D])
        acc1, acc2 = sb("acc1", [P, ACC]), sb("acc2", [P, ACC])
        rel = acc2[:, 4 * CT * P:4 * CT * P + C]
        src_col = sb("src_col", [P, C], i32)
        key_col = sb("key_col", [P, C])
        type_col = sb("type_col", [P, C], bf16)
        w_col = sb("w_col", [P, C])
        base_i = sb("base_i", [1, NG], i32)
        idx = sb("idx", [P, NSLOT], i32)
        rows = sb("rows", [P, NSLOT, D])
        sw = sb("sw", [P, NSLOT])
        window = sb("window", [P, 2, CG, R * W])
        agg = sb("agg", [P, 2, R * W])
        stage = sb("stage", [P, BS, TB * P])
        tile_rows = sb("tile_rows", [P, D])
        tile_T = sb("tile_T", [P, P])
        W1s, W2s = sb("W1s", [P, R, D]), sb("W2s", [P, R, D])
        W3s, W3T = sb("W3s", [P, D]), sb("W3T", [P, 1, D])
        root1s, root2s = sb("root1s", [P, D]), sb("root2s", [P, D])
        b1s, b2s, b3s = sb("b1s", [P, 1]), sb("b2s", [P, 1]), sb("b3s", [P, 1])
        ident = sb("ident", [P, P])
        row0 = sb("row0", [P, P])
        iota = sb("iota", [P, R * P])
        eps = sb("eps", [P, 1])
        stats = sb("stats", [P, STAT, 6])
        mv = sb("mv", [P, STAT, 2])
        std, rstd, shift = sb("std", [P, STAT]), sb("rstd", [P, STAT]), sb("shift", [P, STAT])
        ext = sb("ext", [P, 4])
        extg = sb("extg", [P, 4])
        wscale = sb("wscale", [P, 1])
        small = sb("small", [1, 4])
        flag = sb("flag", [1, 1], i32)
        gwindow = window[:, :, :, :].rearrange("p a c w -> p (a c w)")[:, 0:R * P]
        gagg = stage[:, 0, :]
        gtmp = sb("gtmp", [P, 8])

        bank = [ctx.enter_context(nc.psum_tensor(f"bank{k}", [P, 512], fp32)) for k in range(8)]
        agg_ps, mix_ps, turn_ps, root_ps = bank[0:2], bank[2:4], bank[4], bank[5]
        batch_ps = bank[4:8]
        base_ps, w3_ps = bank[0], bank[1]

        s_list = [sem(f"s_list{k}") for k in range(4)]
        s_lists_go = sem("s_lists_go")
        s_weights = sem("s_weights")
        s_pad = sem("s_pad")
        s_const = sem("s_const")
        s_cast = sem("s_cast")
        s_zero = sem("s_zero")
        s_turned = sem("s_turned")
        s_copied_d, s_copied_a = sem("s_copied_d"), sem("s_copied_a")
        s_base, s_base_i = sem("s_base"), sem("s_base_i")
        s_ext, s_extg = sem("s_ext"), sem("s_extg")
        s_flag = sem("s_flag")
        s_w3, s_w3c = sem("s_w3"), sem("s_w3c")
        s_step, s_gstep = sem("s_step"), sem("s_gstep")
        s_key = sem("s_key")
        s_x = [sem("s_x0"), sem("s_x1")]
        s_store = sem("s_store")
        s_stats, s_mv, s_std, s_rstd, s_shift = (
            sem(n) for n in ("s_stats", "s_mv", "s_std", "s_rstd", "s_shift"))
        s_norm = sem("s_norm")
        s_staged, s_batch, s_out = sem("s_staged"), sem("s_batch"), sem("s_out")
        s_idx, s_sw, s_window = sem("s_idx"), sem("s_sw"), sem("s_window")
        s_row = [sem(f"s_row{k}") for k in range(NSLOT)]
        s_agg, s_agg_sb, s_mix, s_acc = (
            sem(n) for n in ("s_agg", "s_agg_sb", "s_mix", "s_acc"))
        s_tile, s_tileT, s_tile_sb, s_root, s_own = (
            sem(n) for n in ("s_tile", "s_tileT", "s_tile_sb", "s_root", "s_own"))
        s_round = sem("s_round")
        s_gidx, s_grow = sem("s_gidx"), sem("s_grow")
        s_gs, s_gwindow, s_gagg, s_gagg_sb, s_gmix, s_gacc = (
            sem(n) for n in ("s_gs", "s_gwindow", "s_gagg", "s_gagg_sb", "s_gmix", "s_gacc"))
        s_hold = sem("s_hold")

        def wait(eng, s, v):
            if isinstance(v, int) and v <= 0:
                return
            eng.wait_ge(s, v)

        def hold(eng):
            eng.sem_inc(s_hold)

        def first(b, n):
            return isinstance(b, int) and b < n

        def iterations(eng, n, body):
            body(0)
            if n > 2:
                with eng.Fori(1, n - 1) as i:
                    body(i)
            if n > 1:
                body(n - 1)

        def portions(eng, size, slots, step):
            n = -(-NT // size)
            whole = (n - 1) // slots
            for b in range(min(slots, n)):
                step(b, b, min(size, NT - b * size))
            if whole > 1:
                with eng.Fori(1, whole) as i:
                    for s in range(slots):
                        step(i * slots + s, s, size)
            for b in range(max(whole, 1) * slots, n):
                step(b, b % slots, min(size, NT - b * size))

        def sections(eng, step):
            portions(eng, TS, SS, step)

        def batches(eng, step):
            portions(eng, TB, BS, step)

        def over_groups(eng, group):
            def body(i):
                for q in range(GI):
                    g = i * GI + q
                    if not isinstance(g, int):
                        group(i, g, q, CG)
                    elif g < NG:
                        group(i, g, q, min(CG, C - g * CG))
            iterations(eng, NI, body)

        def columns(t, b, size, n):
            return t[:, bass.ds(b * (size * P), n * P)]

        def move_rows(eng, dram, b, size, n, store, signal):
            parts = [(n, P)]
            if dram.shape[0] == N and split_last and isinstance(b, int) and b * size + n == NT:
                parts = [(n - 1, P), (1, last_rows)]
            done = 0
            for k, r in parts:
                if k:
                    d = dram[bass.ds(b * (size * P) + done * P, k * P if r == P else r), :]
                    d = d.rearrange("(t p) d -> p t d", p=r)
                    t = node[0:r, bass.ds(b * (size * D) + done * D, k * D)].rearrange("p (t d) -> p t d", d=D)
                    eng.dma_start(*((d, t) if store else (t, d))).then_inc(signal, 16)
                done += k

        def moves(n):
            return 2 if split_last and n > 1 else 1

        last_section, last_batch = NT - (NS - 1) * TS, NT - (NB - 1) * TB
        stored = [16 * NS, 16 * (NS + NB), 16 * (NS + 2 * NB)]
        stored_all = stored[2] + 16 * (NB - 1 + moves(last_batch))

        def row_base(r, slot):
            return 16 * r * (NI - 1 + (slot < last_chunks))

        block = ctx.enter_context(nc.Block())

        @block.sync
        def _(eng):
            eng.wait_ge(s_pad, 1)

            def section(b, s, n):
                if not first(b, SS):
                    eng.wait_ge(s_x[s], b * 8 - 8 * s)
                move_rows(eng, x, b, TS, n, False, s_x[s])
                if isinstance(b, int) and b == min(1, NS - 1):
                    eng.sem_inc(s_lists_go)
            sections(eng, section)

            def section_out(b, s, n):
                eng.wait_ge(s_norm, b + 1)
                move_rows(eng, table[0], b, TS, n, True, s_store)
            sections(eng, section_out)

            def own_hidden(i):
                wait(eng, s_tileT, i)
                eng.dma_start(tile_rows[:, :], table[0][bass.ds(i * P, P), :]).then_inc(s_tile, 16)
            eng.wait_ge(s_store, stored[0])
            iterations(eng, NT, own_hidden)

            def hidden_out(b, s, n):
                eng.wait_ge(s_out, b + 1)
                move_rows(eng, table[1], b, TB, n, True, s_store)
            batches(eng, hidden_out)

            def own_x(i):
                wait(eng, s_root, i + NT)
                r = last_rows if isinstance(i, int) and i == NT - 1 else P
                eng.dma_start(tile_rows[0:r, :], x[bass.ds(i * P, r), :]).then_inc(s_tile, 16)
            iterations(eng, NT, own_x)

            def normal_out(b, s, n):
                eng.wait_ge(s_norm, b + (NS + 1))
                move_rows(eng, table[2], b, TB, n, True, s_store)
            batches(eng, normal_out)

            def result_out(b, s, n):
                eng.wait_ge(s_out, b + (NB + 1))
                move_rows(eng, out, b, TB, n, True, s_store)
            batches(eng, result_out)
            eng.wait_ge(s_store, stored_all)

        @block.gpsimd
        def _(eng):
            eng.memset(ident[:, :], 0.0).then_inc(s_const, 1)
            eng.memset(row0[:, :], 0.0).then_inc(s_const, 1)
            eng.memset(eps[:, :], LN_EPS).then_inc(s_const, 1)
            eng.wait_ge(s_const, 2)
            eng.affine_select(out=ident[:, :], in_=ident[:, :], compare_op=ALU.not_equal, fill=1.0,
                              base=0, pattern=[[-1, P]], channel_multiplier=1).then_inc(s_const, 1)
            eng.memset(row0[0:1, :], 1.0).then_inc(s_const, 1)
            eng.iota(iota[:, :], [[1, R * P]], base=0, channel_multiplier=0,
                     allow_small_or_imprecise_dtypes=True).then_inc(s_const, 1)
            eng.memset(acc1[:, :], 0.0).then_inc(s_zero, 1)
            eng.wait_ge(s_ext, 1)
            eng.partition_all_reduce(extg[:, :], ext[:, :], P, REDUCE_MAX).then_inc(s_extg, 1)

            eng.wait_ge(s_flag, 1)
            narrow = eng.value_load(flag[0:1, 0:1], min_val=0, max_val=1)

            def gather(r, slot, signal):
                eng.indirect_dma_start(
                    out=rows[:, slot, :], out_offset=None, in_=table[r][:, :],
                    in_offset=bass.IndirectOffsetOnAxis(ap=idx[:, slot:slot + 1], axis=0)).then_inc(signal, 16)

            def fast(r):
                def group(i, g, q, n):
                    eng.wait_ge(s_idx, g + (r * NG + 1))
                    hold(eng)
                    for k in range(q * CG, q * CG + n):
                        gather(r, k, s_row[k])
                over_groups(eng, group)

            def general(r):
                with eng.Fori(0, C) as c:
                    eng.wait_ge(s_gidx, c + (r * C + 1))
                    hold(eng)
                    gather(r, 0, s_grow)

            for r in range(3):
                eng.wait_ge(s_store, stored[r])
                with eng.If(narrow == 1):
                    fast(r)
                with eng.Else():
                    general(r)

        @block.scalar
        def _(eng):
            eng.wait_ge(s_lists_go, 1)
            lists = [acc2[:, a * CT * P:(a + 1) * CT * P] for a in range(4)]
            full = (CT - 1) * P
            rest = C - full - 1
            for a, arr in enumerate((src, dst, etype, weight)):
                to = lists[a] if arr is weight else lists[a].bitcast(i32)
                if CT > 1:
                    eng.dma_start(to[:, 0:full].rearrange("p (t e) -> p t e", e=P),
                                  arr[0:full * P].rearrange("(t p e) -> p t e", p=P, e=P)).then_inc(s_list[a], 16)
                if rest:
                    eng.dma_start(to[0:rest, full:full + P],
                                  arr[full * P:(C - 1) * P].rearrange("(p e) -> p e", e=P)).then_inc(s_list[a], 16)
                eng.dma_start(to[rest:rest + 1, full:full + tail_edges],
                              arr[(C - 1) * P:E].rearrange("(p e) -> p e", p=1)).then_inc(s_list[a], 16)
                if tail_edges < P:
                    eng.dma_start(to[rest:rest + 1, full + tail_edges:full + P],
                                  arr[E - (P - tail_edges):E].rearrange("(p e) -> p e", p=1)).then_inc(s_list[a], 16)
            weights = ((W3s[:, :], W3), (W1s[:, :, :], W1.rearrange("r f o -> f r o")),
                       (W2s[:, :, :], W2.rearrange("r f o -> f r o")), (root1s[:, :], root1), (root2s[:, :], root2),
                       (b1s[:, :], b1.rearrange("(p a) -> p a", a=1)), (b2s[:, :], b2.rearrange("(p a) -> p a", a=1)),
                       (b3s[:, :], b3.rearrange("(p a) -> p a", a=1)))
            assert len(weights) == N_WEIGHTS
            for to, fr in weights:
                eng.dma_start(to, fr).then_inc(s_weights, 16)
            def root_of_var(base, b, size, slots, s, n):
                eng.wait_ge(s_mv, b + (base + 1))
                wait(eng, s_shift, b + (base - slots + 1))
                eng.activation(std[:, s * size:s * size + n], mv[:, s * size:s * size + n, 1], ACT.Sqrt,
                               bias=eps[:, 0:1]).then_inc(s_std, 1)

            def normalise(base, b, size, slots, s, n, source):
                eng.wait_ge(s_shift, b + (base + 1))
                for t in range(n):
                    k = s * size + t
                    ins = eng.activation(columns(node, b * size + t, 1, 1), source(b, s, t), ACT.Relu,
                                         bias=shift[:, k:k + 1], scale=rstd[:, k:k + 1])
                ins.then_inc(s_norm, 1)

            eng.wait_ge(s_const, N_CONST)

            def of_x(b, s, t):
                return columns(node, b * TS + t, 1, 1)

            def cast_lists():
                for a in range(3):
                    eng.wait_ge(s_list[a], 16 * LIST_LOADS)
                    if CT > 1:
                        eng.activation(lists[a][:, 0:full], lists[a][:, 0:full].bitcast(i32), ACT.Copy)
                    part = lists[a][0:rest + 1, full:full + P]
                    eng.activation(part, part.bitcast(i32), ACT.Copy).then_inc(s_cast, 1)

            def copy_lists():
                for n in range(2 * MB, 4 * MB):
                    a, t = divmod(n, MB)
                    w = min(512, C - t * 512)
                    eng.wait_ge(s_turned, n + 1)
                    eng.activation((type_col if a == 2 else w_col)[:, t * 512:t * 512 + w], batch_ps[n % 4][:, 0:w],
                                   ACT.Copy).then_inc(s_copied_a, 1)

            def section(b, s, n):
                root_of_var(0, b, TS, SS, s, n)
                if isinstance(b, int) and b == 0:
                    cast_lists()
                if isinstance(b, int) and b == min(1, NS - 1):
                    copy_lists()
                if not first(b, 1):
                    normalise(0, b - 1, TS, SS, (s - 1) % SS, TS, of_x)
            sections(eng, section)
            normalise(0, NS - 1, TS, SS, (NS - 1) % SS, last_section, of_x)

            eng.wait_ge(s_flag, 1)
            narrow = eng.value_load(flag[0:1, 0:1], min_val=0, max_val=1)

            def own(r, i):
                wait(eng, s_root, i + r * NT)
                if r == 0:
                    eng.wait_ge(s_tileT, i + 1)
                    eng.activation(tile_T[:, :], turn_ps[:, 0:P], ACT.Copy).then_inc(s_tile_sb, 1)
                else:
                    eng.activation(tile_T[:, :], columns(acc1, i, 1, 1), ACT.Relu).then_inc(s_tile_sb, 1)

            def fast(r):
                width = R * W if r < 2 else W

                def group(i, g, q, n):
                    if q == 0 and r < 2:
                        own(r, i)
                    eng.wait_ge(s_agg, g + (r * NG + 1))
                    wait(eng, s_mix, g + (r * NG - 1))
                    eng.activation(agg[:, q % 2, 0:width], agg_ps[q % 2][:, 0:width], ACT.Copy).then_inc(s_agg_sb, 1)
                over_groups(eng, group)

            def general(r):
                if r < 2:
                    iterations(eng, NT, lambda i: own(r, i))
                width = R * P if r < 2 else P
                with eng.Fori(0, C) as c:
                    with eng.Fori(0, NT) as v:
                        eng.wait_ge(s_gagg, c * NT + v + (r * C * NT + 1))
                        eng.activation(gagg[:, 0:width], agg_ps[0][:, 0:width], ACT.Copy).then_inc(s_gagg_sb, 1)

            eng.wait_ge(s_key, 1)
            eng.memzero(acc2[:, :]).then_inc(s_zero, 1)
            for r in range(3):
                with eng.If(narrow == 1):
                    fast(r)
                with eng.Else():
                    general(r)
                if r == 1:
                    def norm_batch(b, s, n):
                        root_of_var(NS, b, TB, BS, s, n)
                        if not first(b, 1):
                            normalise(NS, b - 1, TB, BS, (s - 1) % BS, TB, of_psum)

                    def of_psum(b, s, t):
                        return batch_ps[s][:, t * D:(t + 1) * D]
                    batches(eng, norm_batch)
                    normalise(NS, NB - 1, TB, BS, (NB - 1) % BS, last_batch, of_psum)
                else:
                    def copy_out(b, s, n):
                        eng.wait_ge(s_batch, b + ((0, 0, 2 * NB)[r] + 1))
                        eng.activation(columns(node, b, TB, n), batch_ps[s][:, 0:n * D],
                                       ACT.Relu if r == 0 else ACT.Copy).then_inc(s_out, 1)
                    batches(eng, copy_out)

        @block.tensor
        def _(eng):
            eng.wait_ge(s_const, N_CONST)
            for n in range(4 * MB):
                a, t4 = divmod(n, MB)
                if n == 2 * MB:
                    eng.wait_ge(s_copied_d, 2 * MB)
                    eng.matmul(base_ps[:, 0:NG], row0[:, :], key_col[:, 0:C:CG], start=True, stop=True).then_inc(s_base, 1)
                if t4 == 0:
                    eng.wait_ge(*((s_cast, a + 1) if a < 3 else (s_list[3], 16 * LIST_LOADS)))
                if n >= 4:
                    wait(eng, s_copied_d, min(n - 3, 2 * MB))
                    wait(eng, s_copied_a, n - 3 - 2 * MB)
                for t in range(4 * t4, min(4 * t4 + 4, CT)):
                    k = min(P, C - t * P)
                    lo = a * CT * P + t * P
                    ins = eng.transpose(batch_ps[n % 4][:, (t % 4) * P:(t % 4) * P + k], acc2[0:k, lo:lo + P],
                                        ident[0:k, 0:k])
                ins.then_inc(s_turned, 1)
            eng.wait_ge(s_weights, 16 * N_WEIGHTS)
            eng.transpose(w3_ps[:, 0:P], W3s[:, :], ident[:, :]).then_inc(s_w3, 1)

            eng.wait_ge(s_flag, 1)
            narrow = eng.value_load(flag[0:1, 0:1], min_val=0, max_val=1)
            eng.wait_ge(s_w3c, 1)

            def own_turn(i):
                eng.wait_ge(s_tile, i * 16 + 16)
                wait(eng, s_tile_sb, i)
                eng.transpose(turn_ps[:, 0:P], tile_rows[:, :], ident[:, :]).then_inc(s_tileT, 1)

            def own_root(r, i):
                eng.wait_ge(s_tile_sb, i + (r * NT + 1))
                wait(eng, s_own, i + r * NT)
                if r == 0:
                    eng.matmul(root_ps[:, 0:P], root1s[:, :], tile_T[:, :], start=True, stop=True).then_inc(s_root, 1)
                else:
                    eng.matmul(root_ps[:, 0:P], root2s[:, :], tile_T[:, :], start=True, stop=False)
                    eng.wait_ge(s_tile, (i + NT) * 16 + 16)
                    eng.matmul(root_ps[:, 0:P], tile_rows[:, :], ident[:, :], start=False, stop=True).then_inc(s_root, 1)

            relations = (W1s, W2s, W3T)

            def mix(r, ps, sums, w):
                nr = relations[r].shape[1]
                for k in range(nr):
                    ins = eng.matmul(ps[:, 0:w], relations[r][:, k, :], sums[:, k * w:(k + 1) * w],
                                     start=(k == 0), stop=(k == nr - 1))
                return ins

            def fast(r):
                width = R * W if r < 2 else W

                def mix_group(g, q):
                    eng.wait_ge(s_agg_sb, g + (r * NG + 1))
                    if not first(g, 2):
                        eng.wait_ge(s_acc, g + (r * NG - 1))
                    mix(r, mix_ps[q % 2], agg[:, q % 2, :], W).then_inc(s_mix, 1)

                def group(i, g, q, n):
                    eng.wait_ge(s_window, g + (r * NG + 1))
                    if not first(g, 2):
                        eng.wait_ge(s_agg_sb, g + (r * NG - 1))
                    for k in range(n):
                        slot = q * CG + k
                        eng.wait_ge(s_row[slot], i * 16 + (row_base(r, slot) + 16))
                        ins = eng.matmul(agg_ps[q % 2][:, 0:width], rows[:, slot, :], window[:, q % 2, k, 0:width],
                                         start=(k == 0), stop=(k == n - 1))
                    ins.then_inc(s_agg, 1)
                    if not first(g, 1):
                        mix_group(g - 1, q - 1 + GI)
                    if q == 0 and r == 0:
                        own_turn(i)
                    if q == 1 and r < 2:
                        own_root(r, i)
                over_groups(eng, group)
                mix_group(NG - 1, (NG - 1) % GI)

            def general(r):
                if r < 2:
                    def own(i):
                        if r == 0:
                            own_turn(i)
                        own_root(r, i)
                    iterations(eng, NT, own)
                width = R * P if r < 2 else P
                with eng.Fori(0, C) as c:
                    eng.wait_ge(s_grow, c * 16 + (r * C * 16 + 16))
                    hold(eng)
                    with eng.Fori(0, NT) as v:
                        event = c * NT + v + (r * C * NT + 1)
                        eng.wait_ge(s_gwindow, event)
                        eng.matmul(agg_ps[0][:, 0:width], rows[:, 0, :], gwindow[:, 0:width],
                                   start=True, stop=True).then_inc(s_gagg, 1)
                        eng.wait_ge(s_gagg_sb, event)
                        mix(r, mix_ps[0], gagg, P).then_inc(s_gmix, 1)

            def turn(r, b, s, n):
                eng.wait_ge(s_staged, b + (r * NB + 1))
                if r == 1:
                    wait(eng, s_norm, b + (NS - BS + 1) if not first(b, BS) else 0)
                else:
                    wait(eng, s_out, b + ((0, 0, NB)[r] - BS + 1) if not first(b, BS) else 0)
                for t in range(n):
                    ins = eng.transpose(batch_ps[s][:, t * P:(t + 1) * P], stage[:, s, t * P:(t + 1) * P], ident[:, :])
                ins.then_inc(s_batch, 1)

            for r in range(3):
                with eng.If(narrow == 1):
                    fast(r)
                with eng.Else():
                    general(r)
                batches(eng, lambda b, s, n: turn(r, b, s, n))

        @block.vector
        def _(eng):
            steps = {s_step: 0, s_gstep: 0}

            def link(ins, s=s_step):
                steps[s] += 1
                ins.then_inc(s, 1)
                eng.wait_ge(s, steps[s])

            pad = 96 if last_rows >= 96 else last_rows // 64 * 64
            eng.memset(node[pad:P, (NT - 1) * D:NT * D], 0.0).then_inc(s_pad, 1)
            def statistics(base, b, size, slots, s, n, source):
                wait(eng, s_mv, b + (base - slots + 1))
                hold(eng)
                for t in range(n):
                    ins = eng.bn_stats(stats[:, s * size + t, :], source(b, s, t))
                ins.then_inc(s_stats, 1)
                eng.wait_ge(s_stats, b + (base + 1))
                wait(eng, s_shift, b + (base - slots + 1))
                hold(eng)
                for t in range(n):
                    ins = eng.bn_aggr(mv[:, s * size + t, :], stats[:, s * size + t, :])
                ins.then_inc(s_mv, 1)

            def scale_and_shift(base, b, size, slots, s, n):
                c = slice(s * size, s * size + n)
                eng.wait_ge(s_std, b + (base + 1))
                wait(eng, s_norm, b + (base - slots + 1))
                eng.reciprocal(rstd[:, c], std[:, c]).then_inc(s_rstd, 1)
                eng.wait_ge(s_rstd, b + (base + 1))
                eng.scalar_tensor_tensor(out=shift[:, c], in0=mv[:, c, 0], scalar=-1.0, in1=rstd[:, c],
                                         op0=ALU.mult, op1=ALU.mult).then_inc(s_shift, 1)

            def edge_lists():
                for n in range(2 * MB):
                    a, t = divmod(n, MB)
                    w = min(512, C - t * 512)
                    eng.wait_ge(s_turned, n + 1)
                    eng.tensor_copy((src_col if a == 0 else key_col)[:, t * 512:t * 512 + w],
                                    batch_ps[n % 4][:, 0:w]).then_inc(s_copied_d, 1)
                eng.wait_ge(s_base, 1)
                eng.tensor_copy(base_i[0:1, :], base_ps[0:1, 0:NG]).then_inc(s_base_i, 1)
                eng.wait_ge(s_copied_d, 2 * MB)
                gf = C // CG
                cf = gf * CG
                link(eng.tensor_tensor(
                    rel[:, 0:cf].rearrange("p (g j) -> p g j", j=CG), key_col[:, 0:cf].rearrange("p (g j) -> p g j", j=CG),
                    base_ps[:, 0:gf].unsqueeze(2).to_broadcast([P, gf, CG]), ALU.subtract))
                if C > cf:
                    link(eng.tensor_scalar(rel[:, cf:C], key_col[:, cf:C], base_ps[:, gf:gf + 1], None, ALU.subtract))
                eng.tensor_reduce(ext[:, 0:1], rel, axis=AX, op=ALU.max)
                link(eng.tensor_reduce(ext[:, 1:2], rel, axis=AX, op=ALU.min))
                eng.wait_ge(s_copied_a, 2 * MB)
                eng.tensor_reduce(ext[:, 2:3], w_col[:, :], axis=AX, op=ALU.max)
                link(eng.tensor_reduce(ext[:, 3:4], w_col[:, :], axis=AX, op=ALU.min))
                eng.tensor_scalar(ext[:, 1:4:2], ext[:, 1:4:2], -1.0, None, ALU.mult).then_inc(s_ext, 1)

            def section(b, s, n):
                whole = b * 8 + (16 - 8 * s)
                last = isinstance(b, int) and b == NS - 1
                eng.wait_ge(s_x[s], whole + (16 * (moves(n) - 1) if last else 0))
                statistics(0, b, TS, SS, s, n, lambda b, s, t: columns(node, b * TS + t, 1, 1))
                if isinstance(b, int) and b == min(1, NS - 1):
                    edge_lists()
                if not first(b, 1):
                    scale_and_shift(0, b - 1, TS, SS, (s - 1) % SS, TS)
            sections(eng, section)
            scale_and_shift(0, NS - 1, TS, SS, (NS - 1) % SS, last_section)

            eng.wait_ge(s_extg, 1)
            link(eng.tensor_tensor(wscale[:, :], extg[:, 2:3], extg[:, 3:4], ALU.add))
            link(eng.tensor_scalar(wscale[:, :], wscale[:, :], RANGE_EPS, None, ALU.add))
            link(eng.reciprocal(wscale[:, :], wscale[:, :]))
            link(eng.tensor_scalar(small[:, 0:1], extg[0:1, 0:1], float(W), None, ALU.is_lt))
            link(eng.tensor_scalar(small[:, 1:2], extg[0:1, 1:2], 0.0, None, ALU.is_le))
            link(eng.tensor_tensor(small[:, 2:3], small[:, 0:1], small[:, 1:2], ALU.mult))
            eng.tensor_copy(flag[:, :], small[:, 2:3]).then_inc(s_flag, 1)
            eng.wait_ge(s_w3, 1)
            eng.tensor_copy(W3T[:, 0, :], w3_ps[:, 0:P]).then_inc(s_w3c, 1)
            eng.wait_ge(s_base_i, 1)
            eng.wait_ge(s_flag, 1)
            narrow = eng.value_load(flag[0:1, 0:1], min_val=0, max_val=1)

            def no_pads(s):
                if tail_edges < P:
                    link(eng.memset(key_col[tail_edges:P, C - 1:C], -1.0), s)

            acc_of = (acc1, acc2, acc2)
            bias_of = (b1s, b2s, b3s)

            def own(r, i):
                a = columns(acc_of[r], i, 1, 1)
                if r < 2:
                    eng.wait_ge(s_root, i + (r * NT + 1))
                    eng.scalar_tensor_tensor(out=a, in0=root_ps[:, 0:P], scalar=bias_of[r][:, 0:1], in1=a,
                                             op0=ALU.add, op1=ALU.add).then_inc(s_own, 1)
                else:
                    eng.tensor_scalar(a, a, bias_of[r][:, 0:1], None, ALU.add).then_inc(s_own, 1)

            def fast(r):
                width = R * W if r < 2 else W
                T = r * NG

                def scale_weights(c, k, m):
                    eng.tensor_scalar(sw[:, k:k + m], w_col[:, bass.ds(c, m)], extg[:, 3:4], wscale[:, 0:1],
                                      ALU.add, ALU.mult).then_inc(s_sw, 1)
                for q in range(GI):
                    eng.tensor_copy(idx[:, q * CG:(q + 1) * CG], src_col[:, q * CG:(q + 1) * CG]).then_inc(s_idx, 1)
                for q in range(GI):
                    if r < 2:
                        scale_weights(q * CG, q * CG, CG)
                if r == 0:
                    link(eng.scalar_tensor_tensor(out=key_col[:, :], in0=type_col[:, :], scalar=float(W), in1=rel,
                                                  op0=ALU.mult, op1=ALU.add))
                    no_pads(s_step)
                elif r == 2:
                    link(eng.scalar_tensor_tensor(out=key_col[:, :], in0=type_col[:, :], scalar=-float(W),
                                                  in1=key_col[:, :], op0=ALU.mult, op1=ALU.add))
                    no_pads(s_step)
                if r == 0:
                    eng.sem_inc(s_key)

                def add_window(g, q):
                    base = eng.value_load(base_i[0:1, bass.ds(g, 1)], min_val=0, max_val=N - 1)
                    a = acc_of[r][:, bass.ds(base, W)]
                    eng.wait_ge(s_mix, g + (T + 1))
                    wait(eng, s_acc, g + T)
                    eng.tensor_tensor(a, a, mix_ps[q % 2][:, 0:W], ALU.add).then_inc(s_acc, 1)

                def group(i, g, q, n):
                    if not first(g, 2):
                        eng.wait_ge(s_agg, g + (T - 1))
                        if not (isinstance(g, int) and g + 2 >= NG):
                            m = min(CG, C - (g + 2) * CG) if isinstance(g, int) else CG
                            k = ((q + 2) % GI) * CG
                            eng.tensor_copy(idx[:, k:k + m], src_col[:, bass.ds(g * CG + 2 * CG, m)]).then_inc(s_idx, 1)
                            if r < 2:
                                scale_weights(g * CG + 2 * CG, k, m)
                    if r < 2:
                        eng.wait_ge(s_sw, g + (T + 1))
                    for k in range(n):
                        c = q * CG + k
                        wt = sw[:, c:c + 1] if r < 2 else w_col[:, bass.ds(i * NSLOT + c, 1)]
                        ins = eng.tensor_scalar(window[:, q % 2, k, 0:width], iota[:, 0:width],
                                                key_col[:, bass.ds(i * NSLOT + c, 1)], wt, ALU.is_equal, ALU.mult)
                    ins.then_inc(s_window, 1)
                    if not first(g, 2):
                        add_window(g - 2, q)
                    if q == 2:
                        eng.wait_ge(s_acc, g + (T - 1))
                        own(r, i)
                        eng.wait_ge(s_own, i + (r * NT + 1))
                eng.wait_ge(s_zero, min(r + 1, 2))
                over_groups(eng, group)
                add_window(NG - 2, (NG - 2) % GI)
                add_window(NG - 1, (NG - 1) % GI)
                eng.wait_ge(s_acc, T + NG)

            def general(r):
                width = R * P if r < 2 else P
                if r == 0:
                    no_pads(s_gstep)
                    eng.sem_inc(s_key)
                eng.wait_ge(s_zero, min(r + 1, 2))
                if r == 2:
                    eng.wait_ge(s_batch, 2 * NB)
                iterations(eng, NT, lambda i: own(r, i))
                eng.wait_ge(s_own, (r + 1) * NT)
                pre, per = 3, 8
                with eng.Fori(0, C) as c:
                    key, start, at, ok, ty, wt = (gtmp[:, k:k + 1] for k in range(6))
                    done = (c + r * C) * (NT * per + pre)
                    eng.tensor_copy(idx[:, 0:1], src_col[:, bass.ds(c, 1)]).then_inc(s_gidx, 1)
                    eng.memset(start, 0.0).then_inc(s_gs, 1)
                    eng.tensor_scalar(ty, type_col[:, bass.ds(c, 1)], float(P), 1.0, ALU.mult, ALU.add).then_inc(s_gs, 1)
                    if r < 2:
                        eng.tensor_scalar(wt, w_col[:, bass.ds(c, 1)], extg[:, 3:4], wscale[:, 0:1],
                                          ALU.add, ALU.mult).then_inc(s_gs, 1)
                    else:
                        eng.tensor_copy(wt, w_col[:, bass.ds(c, 1)]).then_inc(s_gs, 1)
                    with eng.Fori(0, NT) as v:
                        event = c * NT + v + (r * C * NT + 1)
                        so_far = done + v * per + pre
                        eng.wait_ge(s_gs, so_far)
                        eng.tensor_tensor(at, key_col[:, bass.ds(c, 1)], start, ALU.subtract).then_inc(s_gs, 1)
                        eng.wait_ge(s_gs, so_far + 1)
                        eng.tensor_scalar(ok, at, 0.0, None, ALU.is_ge).then_inc(s_gs, 1)
                        eng.tensor_scalar(key, at, float(P), None, ALU.is_lt).then_inc(s_gs, 1)
                        eng.wait_ge(s_gs, so_far + 3)
                        eng.tensor_tensor(ok, ok, key, ALU.mult).then_inc(s_gs, 1)
                        if r < 2:
                            eng.tensor_tensor(at, at, ty, ALU.add).then_inc(s_gs, 1)
                        else:
                            eng.tensor_scalar(at, at, 1.0, None, ALU.add).then_inc(s_gs, 1)
                        eng.wait_ge(s_gs, so_far + 5)
                        eng.tensor_tensor(at, at, ok, ALU.mult).then_inc(s_gs, 1)
                        eng.tensor_scalar(start, start, float(P), None, ALU.add).then_inc(s_gs, 1)
                        eng.wait_ge(s_gs, so_far + 7)
                        eng.tensor_scalar(at, at, -1.0, None, ALU.add).then_inc(s_gs, 1)
                        eng.wait_ge(s_gs, so_far + 8)
                        eng.tensor_scalar(gwindow[:, 0:width], iota[:, 0:width], at, wt,
                                          ALU.is_equal, ALU.mult).then_inc(s_gwindow, 1)
                        a = columns(acc_of[r], v, 1, 1)
                        eng.wait_ge(s_gmix, event)
                        eng.tensor_tensor(a, a, mix_ps[0][:, 0:P], ALU.add).then_inc(s_gacc, 1)
                        eng.wait_ge(s_gacc, event)

            for r in range(3):
                with eng.If(narrow == 1):
                    fast(r)
                with eng.Else():
                    general(r)
                eng.sem_inc(s_round)

                def put(b, s, n):
                    wait(eng, s_batch, b + (r * NB - BS + 1))
                    eng.tensor_copy(stage[:, s, 0:n * P], columns(acc_of[r], b, TB, n)).then_inc(s_staged, 1)

                if r != 1:
                    batches(eng, put)
                    continue

                def batch_statistics(b, s, n):
                    eng.wait_ge(s_batch, b + (NB + 1))
                    statistics(NS, b, TB, BS, s, n, lambda b, s, t: batch_ps[s][:, t * D:(t + 1) * D])

                def norm_batch(b, s, n):
                    put(b, s, n)
                    if not first(b, 2):
                        batch_statistics(b - 2, (s - 2) % BS, TB)
                    if not first(b, 3):
                        scale_and_shift(NS, b - 3, TB, BS, (s - 3) % BS, TB)
                batches(eng, norm_batch)
                batch_statistics(NB - 2, (NB - 2) % BS, TB)
                scale_and_shift(NS, NB - 3, TB, BS, (NB - 3) % BS, TB)
                batch_statistics(NB - 1, (NB - 1) % BS, last_batch)
                scale_and_shift(NS, NB - 2, TB, BS, (NB - 2) % BS, TB)
                scale_and_shift(NS, NB - 1, TB, BS, (NB - 1) % BS, last_batch)


N_CONST = 6
N_WEIGHTS = 8


_INS = ['x', 'src', 'dst', 'edge_type_4', 'edge_weight', 'L0_gnn_W1', 'L0_gnn_root1', 'L0_gnn_b1', 'L0_gnn_W2',
        'L0_gnn_root2', 'L0_gnn_b2', 'L1_gnn_W', 'L1_gnn_b']


def kernel(**inputs):
    import numpy as _np
    import concourse.bacc as _bacc
    from concourse import mybir as _mybir
    from concourse.bass_utils import run_bass_kernel_spmd as _run

    nc = _bacc.Bacc("TRN2", target_bir_lowering=False, num_devices=1)
    arrays, args = {}, []
    for name in _INS:
        a = _np.ascontiguousarray(inputs[name])
        arrays[f"in_{name}_dram"] = a
        args.append(nc.dram_tensor(f"in_{name}_dram", a.shape, _mybir.dt.from_np(a.dtype), kind="ExternalInput").ap())
    x = inputs['x']
    args.append(nc.dram_tensor("out_0_dram", tuple(x.shape), _mybir.dt.float32, kind="ExternalOutput").ap())
    build(nc, *args)
    r = _run(nc, [arrays], core_ids=[0])
    return r.results[0]["out_0_dram"]
```
